# Optimizing a Trainium2 kernel written in Bass

```python
import numpy as np
import jax
import jax.numpy as jnp

def _softmax(x, axis=-1):
    return jax.nn.softmax(x, axis=axis)
def _gelu(x):
    return jax.nn.gelu(x, approximate=True)
def _silu(x):
    return jax.nn.silu(x)
def _sigmoid(x):
    return jax.nn.sigmoid(x)
def _layernorm(x, axis=-1, eps=1e-5):
    m = jnp.mean(x, axis=axis, keepdims=True)
    v = jnp.var(x, axis=axis, keepdims=True)
    return (x - m) / jnp.sqrt(v + eps)
def _scatter_add(tgt, idx, src, axis=0):
    return tgt.at[idx].add(src)
def _segment_sum(src, seg, n):
    return jax.ops.segment_sum(src, seg, n)

kernel_name = 'mk_adj_resnorm_d4_adj_256_d4dc5c'

def setup_inputs(seed: int = 0):
    np.random.seed(seed)
    _w = jnp.asarray
    def _rec_inputs():
        import jax
        import jax.numpy as jnp
        _gk = jax.random.key(seed)
        x = -0.0005207 + 1.001 * jax.random.normal(jax.random.fold_in(_gk, 1), (4096, 256), jnp.float32)
        _a = jax.random.bernoulli(jax.random.fold_in(_gk, 2), 0.00390625, (4096, 4096))
        _a = jnp.logical_or(_a, jnp.swapaxes(_a, -1, -2))
        _a = jnp.logical_or(_a, jnp.eye(4096, dtype=bool))
        _af = _a.astype(jnp.float32)
        _af = _af * jax.random.uniform(jax.random.fold_in(_gk, 3), (4096, 4096), jnp.float32, 0.05, 1)
        adj = _af
        return x, adj
    x, adj = _rec_inputs()
    def _L0_gnn_setup():
        import jax, jax.numpy as jnp
        import numpy as np
        N = 8192
        DIM = 256
        HEADS = 4
        HD = DIM // HEADS
        SCALE = HD ** (-0.5)
        key = jax.random.key(seed)
        ks = jax.random.split(key, 8)
        x = jax.random.normal(ks[0], (N, DIM), dtype=jnp.float32)
        adj_matrix = jax.random.uniform(ks[1], (N, N), dtype=jnp.float32)
        attn_mask = jax.random.randint(ks[2], (N, N), 0, 2, dtype=jnp.int32)
        Wqkv = jax.random.normal(ks[3], (DIM, 3 * DIM), dtype=jnp.float32) * DIM ** (-0.5)
        bqkv = jnp.zeros((3 * DIM,), dtype=jnp.float32)
        Wout = jax.random.normal(ks[4], (DIM, DIM), dtype=jnp.float32) * DIM ** (-0.5)
        bout = jnp.zeros((DIM,), dtype=jnp.float32)
        graph_bias = jax.random.normal(ks[5], (1, 1, 1), dtype=jnp.float32) * 0.1
        return {'x': x, 'adj_matrix': adj_matrix, 'attn_mask': attn_mask, 'Wqkv': Wqkv, 'bqkv': bqkv, 'Wout': Wout, 'bout': bout, 'graph_bias': graph_bias}
    _L0_gnn_all = _L0_gnn_setup()
    _L0_gnn_in = {k: v for k, v in _L0_gnn_all.items() if k in ('Wqkv', 'bqkv', 'Wout', 'bout', 'graph_bias', )}
    del _L0_gnn_all

    def _L1_gnn_setup():
        import jax, jax.numpy as jnp
        import numpy as np
        NEG_INF = -9000000000000000.0
        NEG_SLOPE = 0.2
        key = jax.random.key(seed)
        k1, k2, k3, k4 = jax.random.split(key, 4)
        N, d_in, d_out = (8192, 256, 256)
        x = jax.random.normal(k1, (N, d_in), dtype=jnp.float32)
        adj = jax.random.randint(k2, (N, N), 0, 2).astype(jnp.float32)
        W = jax.random.normal(k3, (d_in, d_out), dtype=jnp.float32) * (1.0 / np.sqrt(d_in))
        a = jax.random.normal(k4, (2 * d_out,), dtype=jnp.float32) * (1.0 / np.sqrt(2 * d_out))
        return {'x': x, 'adj': adj, 'W': W, 'a': a}
    _L1_gnn_all = _L1_gnn_setup()
    _L1_gnn_in = {k: v for k, v in _L1_gnn_all.items() if k in ('W', 'a', )}
    del _L1_gnn_all

    def _L2_gnn_setup():
        import jax, jax.numpy as jnp
        import numpy as np
        N = 8192
        F_IN = 256
        F_OUT = 256
        key = jax.random.key(seed)
        k1, k2, k3, k4 = jax.random.split(key, 4)
        x = jax.random.normal(k1, (N, F_IN), dtype=jnp.float32)
        adj = jax.random.uniform(k2, (N, N), dtype=jnp.float32)
        bound = 1.0 / np.sqrt(F_IN)
        W = jax.random.uniform(k3, (F_OUT, F_IN), minval=-bound, maxval=bound, dtype=jnp.float32)
        b = jax.random.uniform(k4, (F_OUT,), minval=-bound, maxval=bound, dtype=jnp.float32)
        return {'x': x, 'adj': adj, 'W': W, 'b': b}
    _L2_gnn_all = _L2_gnn_setup()
    _L2_gnn_in = {k: v for k, v in _L2_gnn_all.items() if k in ('W', 'b', )}
    del _L2_gnn_all

    def _L3_gnn_setup():
        import jax, jax.numpy as jnp
        import numpy as np
        N = 8192
        F_IN = 256
        F_OUT = 256
        key = jax.random.key(seed)
        k1, k2, k3 = jax.random.split(key, 3)
        H = jax.random.normal(k1, (N, F_IN), dtype=jnp.float32)
        A_tilde = jax.random.uniform(k2, (N, N), dtype=jnp.float32)
        limit = np.sqrt(6.0 / (F_IN + F_OUT)).astype(np.float32)
        W = jax.random.uniform(k3, (F_IN, F_OUT), dtype=jnp.float32, minval=-limit, maxval=limit)
        return {'H': H, 'A_tilde': A_tilde, 'W': W}
    _L3_gnn_all = _L3_gnn_setup()
    _L3_gnn_in = {k: v for k, v in _L3_gnn_all.items() if k in ('W', )}
    del _L3_gnn_all

    return {
        "x": x,
        "adj": adj,
        "L0_gnn_Wqkv": _L0_gnn_in["Wqkv"],
        "L0_gnn_bqkv": _L0_gnn_in["bqkv"],
        "L0_gnn_Wout": _L0_gnn_in["Wout"],
        "L0_gnn_bout": _L0_gnn_in["bout"],
        "L0_gnn_graph_bias": _L0_gnn_in["graph_bias"],
        "L1_gnn_W": _L1_gnn_in["W"],
        "L1_gnn_a": _L1_gnn_in["a"],
        "L2_gnn_W": _L2_gnn_in["W"],
        "L2_gnn_b": _L2_gnn_in["b"],
        "L3_gnn_W": _L3_gnn_in["W"],
    }

def reference(x, adj, L0_gnn_Wqkv, L0_gnn_bqkv, L0_gnn_Wout, L0_gnn_bout, L0_gnn_graph_bias, L1_gnn_W, L1_gnn_a, L2_gnn_W, L2_gnn_b, L3_gnn_W):
    import jax
    import jax.numpy as jnp
    def _L0_gnn_ref(x, adj_matrix, attn_mask, Wqkv, bqkv, Wout, bout, graph_bias):
        import jax, jax.numpy as jnp
        import numpy as np
        N = 8192
        DIM = 256
        HEADS = 4
        HD = DIM // HEADS
        SCALE = HD ** (-0.5)
        n, d = x.shape
        qkv = x @ Wqkv + bqkv
        q, k, v = jnp.split(qkv, 3, axis=-1)

        def split_heads(t):
            return t.reshape(n, HEADS, HD).transpose(1, 0, 2)
        qh, kh, vh = (split_heads(q), split_heads(k), split_heads(v))
        scores = jnp.einsum('hnd,hmd->hnm', qh, kh) * SCALE
        scores = scores + graph_bias * adj_matrix[None, :, :]
        scores = jnp.where(attn_mask[None, :, :] == 0, jnp.float32(-1000000000.0), scores)
        attn = jax.nn.softmax(scores, axis=-1)
        out = jnp.einsum('hnm,hmd->hnd', attn, vh)
        out = out.transpose(1, 0, 2).reshape(n, d)
        return out @ Wout + bout

    def _L1_gnn_ref(x, adj, W, a):
        import jax, jax.numpy as jnp
        import numpy as np
        NEG_INF = -9000000000000000.0
        NEG_SLOPE = 0.2
        d_out = W.shape[1]
        Wh = x @ W
        e_src = Wh @ a[:d_out]
        e_dst = Wh @ a[d_out:]
        e = jax.nn.leaky_relu(e_src[:, None] + e_dst[None, :], NEG_SLOPE)
        N = Wh.shape[0]
        mask = (adj > 0) | jnp.eye(N, dtype=bool)
        e = jnp.where(mask, e, NEG_INF)
        alpha = jax.nn.softmax(e, axis=1)
        h = alpha @ Wh
        return h

    def _L2_gnn_ref(x, adj, W, b):
        import jax, jax.numpy as jnp
        import numpy as np
        N = 8192
        F_IN = 256
        F_OUT = 256
        rowsum = adj.sum(axis=1)
        d_inv_sqrt = jnp.power(rowsum, -0.5)
        d_inv_sqrt = jnp.where(jnp.isinf(d_inv_sqrt), 0.0, d_inv_sqrt)
        adj_norm = d_inv_sqrt[:, None] * adj * d_inv_sqrt[None, :]
        h = adj_norm @ x
        return h @ W.T + b

    def _L3_gnn_ref(H, A_tilde, W):
        import jax, jax.numpy as jnp
        import numpy as np
        N = 8192
        F_IN = 256
        F_OUT = 256
        d_inv_sqrt = jnp.sum(A_tilde, axis=1) ** (-0.5)
        A_norm = d_inv_sqrt[:, None] * A_tilde * d_inv_sqrt[None, :]
        H_next = A_norm @ H @ W
        return jax.nn.relu(H_next)

    x = _layernorm(x + _L0_gnn_ref(x, adj, adj, L0_gnn_Wqkv, L0_gnn_bqkv, L0_gnn_Wout, L0_gnn_bout, L0_gnn_graph_bias), axis=-1)
    x = _layernorm(x + _L1_gnn_ref(x, adj, L1_gnn_W, L1_gnn_a), axis=-1)
    x = _layernorm(x + _L2_gnn_ref(x, adj, L2_gnn_W, L2_gnn_b), axis=-1)
    x = _layernorm(x + _L3_gnn_ref(x, adj, L3_gnn_W), axis=-1)
    return x


_drawn_inputs = setup_inputs


def setup_inputs(seed=0):
    import zlib

    import numpy as np

    out = dict(_drawn_inputs(seed))
    spreads = {'L0_gnn_bqkv': (0.0, 0.1), 'L0_gnn_bout': (0.0, 0.1)}
    factors = {}
    for name, (base, spread) in spreads.items():
        noise = np.random.default_rng([zlib.crc32(name.encode()), seed]).standard_normal(out[name].shape)
        drawn = base * np.exp(spread * noise) if base else spread * noise
        out[name] = jnp.asarray(drawn.astype(out[name].dtype))
    for name, factor in factors.items():
        out[name] = (out[name] * factor).astype(out[name].dtype)
    return out
```

```python
from contextlib import ExitStack

import concourse.bass as bass
from concourse import mybir

F32 = mybir.dt.float32
F32R = mybir.dt.float32r
ALU = mybir.AluOpType
ACT = mybir.ActivationFunctionType
AX = mybir.AxisListType

P = 128
N = 4096
D = 256
H = 4
HD = D // H
NT = N // P
DH = D // P
BANK = 512
SCALE = HD ** -0.5
MASKED = -1.0e9
NO_EDGE = -9.0e15
SLOPE = 0.2
EPS = 1e-5
LOWEST = -3.0e38


def wait(eng, sem, value):
    if isinstance(value, int) and value <= 0:
        return
    eng.wait_ge(sem, value)


def wait_apart(eng, sem, value, passed):
    wait(eng, sem, value)
    if not isinstance(value, int):
        eng.sem_inc(passed, 1)


def first_and_rest(eng, count, body):
    body(0)
    with eng.Fori(1, count) as i:
        body(i)


class Space:

    def __init__(self, nc, ctx, phase, cleared=None):
        self.nc, self.ctx, self.phase = nc, ctx, phase
        self.cleared = cleared
        self.semaphores = []

    def sb(self, name, shape, dtype=F32):
        return self.ctx.enter_context(self.nc.sbuf_tensor(f"{self.phase}_{name}", shape, dtype))

    def ps(self, name, shape=(P, BANK)):
        return self.ctx.enter_context(self.nc.psum_tensor(f"{self.phase}_{name}", list(shape), F32))

    def sem(self, name):
        if self.cleared:
            return self.cleared.pop()
        made = self.nc.alloc_semaphore(f"{self.phase}_{name}")
        self.semaphores.append(made)
        return made


def tiles_of(dram):
    return dram.rearrange("(k p) d -> p k d", p=P)


def make_identity(pool, ident, made):
    pool.memset(ident[:], 0.0).then_inc(made, 1)
    pool.wait_ge(made, 1)
    pool.affine_select(out=ident[:], in_=ident[:], compare_op=ALU.not_equal, fill=1.0, base=0,
                       pattern=[[-1, P]], channel_multiplier=1).then_inc(made, 1)


class LayerNorm:

    def __init__(self, space, tiles):
        self.tiles = tiles
        self.stats = space.sb("ln_stats", [P, tiles, 6])
        self.mean_var = space.sb("ln_mean_var", [P, tiles, 2])
        self.var_eps = space.sb("ln_var_eps", [P, tiles])
        self.rstd = space.sb("ln_rstd", [P, tiles])
        self.minus_half = space.sb("ln_minus_half", [P, tiles])
        self.half_made = space.sem("ln_half_made")
        self.passed = space.sem("ln_passed")
        self.stats_done = space.sem("ln_stats_done")
        self.mean_done = space.sem("ln_mean_done")
        self.var_done = space.sem("ln_var_done")
        self.rstd_done = space.sem("ln_rstd_done")
        self.norm_done = space.sem("ln_norm_done")

    def constants(self, pool):
        pool.memset(self.minus_half[:], -0.5).then_inc(self.half_made, 1)

    def statistics(self, dve, y, turn):
        for t in range(self.tiles):
            dve.bn_stats(self.stats[:, t, :], y[:, t, :]).then_inc(self.stats_done, 1)
        wait_apart(dve, self.stats_done, self.tiles * (turn + 1), self.passed)
        for t in range(self.tiles):
            dve.bn_aggr(self.mean_var[:, t, :], self.stats[:, t, :]).then_inc(self.mean_done, 1)
        dve.wait_ge(self.mean_done, self.tiles * (turn + 1))
        dve.tensor_scalar(self.var_eps[:], self.mean_var[:, :, 1], EPS, None, ALU.add)\
           .then_inc(self.var_done, 1)

    def power(self, pool, turn):
        if isinstance(turn, int) and turn == 0:
            pool.wait_ge(self.half_made, 1)
        pool.wait_ge(self.var_done, turn + 1)
        pool.tensor_tensor(self.rstd[:], self.var_eps[:], self.minus_half[:], ALU.pow)\
            .then_inc(self.rstd_done, 1)

    def normalise(self, dve, y, turn):
        dve.wait_ge(self.rstd_done, turn + 1)
        for t in range(self.tiles):
            dve.tensor_scalar(y[:, t, :], y[:, t, :], self.mean_var[:, t, 0:1], self.rstd[:, t:t + 1],
                              ALU.subtract, ALU.mult).then_inc(self.norm_done, 1)


def layer0_keys_values(nc, x, Wqkv, bqkv, kT, v_heads, value_stored):
    CT = 4
    CN = CT * P
    CHUNKS = N // CN
    x_tiles = tiles_of(x)
    w_rows = tiles_of(Wqkv)
    with ExitStack() as ctx:
        sp = Space(nc, ctx, "kv")
        ident = sp.sb("ident", [P, P])
        wk = sp.sb("wk", [P, DH, H, 2 * HD])
        wv = sp.sb("wv", [P, DH, D])
        bk = sp.sb("bk", [P, H])
        bv = sp.sb("bv", [P, D])
        xs = sp.sb("xs", [P, 2, CT, D])
        xT = sp.sb("xT", [P, 2, DH, CN])
        v_out = sp.sb("v_out", [P, 2, CT, D])
        turn_bank = [sp.ps(f"turn{i}") for i in range(DH)]
        key_bank = [sp.ps(f"key{i}") for i in range(2)]
        value_bank = [sp.ps(f"value{i}") for i in range(2)]
        ident_made = sp.sem("ident_made")
        weights_loaded = sp.sem("weights_loaded")
        x_loaded = [sp.sem(f"x_loaded{k}") for k in range(2)]
        x_turned = sp.sem("x_turned")
        xT_ready = [sp.sem(f"xT_ready{i}") for i in range(DH)]
        key_made = sp.sem("key_made")
        key_hi = sp.sem("key_hi")
        key_lo = [sp.sem(f"key_lo{b}") for b in range(2)]
        value_made = [sp.sem(f"value_made{k}") for k in range(2)]
        value_out = [sp.sem(f"value_out{b}") for b in range(2)]
        block = ctx.enter_context(nc.Block())
        WEIGHT_LOADS = 2 * DH + 1 + 2 * H + 1

        @block.sync
        def _(sync):
            for k in range(2):
                sync.dma_start(xs[:, k, :, :], x_tiles[:, k * CT:(k + 1) * CT, :]).then_inc(x_loaded[k], 16)
            for half in range(DH):
                for copy in range(2):
                    sync.dma_start(wk[:, half, :, copy * HD:(copy + 1) * HD],
                                   w_rows[:, half, D:2 * D].rearrange("p (h e) -> p h e", h=H))\
                        .then_inc(weights_loaded, 16)
            sync.dma_start(wv[:], w_rows[:, :, 2 * D:3 * D]).then_inc(weights_loaded, 16)
            for copy in range(2):
                for h in range(H):
                    sync.dma_start(bk[copy * HD:(copy + 1) * HD, h:h + 1],
                                   bqkv[D + h * HD:D + (h + 1) * HD].rearrange("(e o) -> e o", o=1))\
                        .then_inc(weights_loaded, 16)
            sync.dma_start(bv[:], bqkv[2 * D:3 * D].rearrange("(a d) -> a d", a=1).to_broadcast([P, D]))\
                .then_inc(weights_loaded, 16)
            with sync.Fori(0, CHUNKS // 2 - 1) as i:
                for k in range(2):
                    u = 2 * i + k
                    sync.wait_ge(x_turned, DH * (u + 1))
                    sync.dma_start(xs[:, k, :, :], x_tiles[:, bass.ds((u + 2) * CT, CT), :])\
                        .then_inc(x_loaded[k], 16)
            for k in range(2):
                sync.wait_ge(value_stored[k], 16 * H * CHUNKS // 2)

        @block.gpsimd
        def _(pool):
            make_identity(pool, ident, ident_made)
            with pool.Fori(0, CHUNKS // 2) as i:
                for k in range(2):
                    u = 2 * i + k
                    for b in range(2):
                        pool.wait_ge(value_out[b], CT // 2 * (u + 1))
                    for h in range(H):
                        pool.dma_start(v_heads[h, :, bass.ds(u * CT, CT), :],
                                       v_out[:, k, :, h * HD:(h + 1) * HD]).then_inc(value_stored[k], 16)

        @block.tensor
        def _(pe):
            pe.wait_ge(ident_made, 2)
            pe.wait_ge(weights_loaded, 16 * WEIGHT_LOADS)
            def body(i):
                for k in range(2):
                    u = 2 * i + k
                    wait(pe, x_loaded[k], 16 * (i + 1))
                    for half in range(DH):
                        wait(pe, xT_ready[half], u)
                        for t in range(CT):
                            last = pe.transpose(turn_bank[half][:, t * P:(t + 1) * P],
                                                xs[:, k, t, half * P:(half + 1) * P], ident[:])
                        last.then_inc(x_turned, 1)
                    for half in range(DH):
                        wait(pe, xT_ready[half], u + 1)
                    for h in range(H):
                        b = h % 2
                        wait(pe, key_lo[b], H // 2 * u + h // 2)
                        for half in range(DH):
                            last = pe.matmul(key_bank[b][:], wk[:, half, h, :], xT[:, k, half, :],
                                             start=half == 0, stop=half == DH - 1)
                        last.then_inc(key_made, 1)
                    for t in range(CT):
                        b = t % 2
                        wait(pe, value_out[b], CT // 2 * u + t // 2)
                        for half in range(DH):
                            last = pe.matmul(value_bank[b][:, 0:D], xT[:, k, half, t * P:(t + 1) * P],
                                             wv[:, half, :], start=half == 0, stop=half == DH - 1)
                        last.then_inc(value_made[k], 1)
            first_and_rest(pe, CHUNKS // 2, body)

        @block.scalar
        def _(act):
            act.wait_ge(weights_loaded, 16 * WEIGHT_LOADS)
            def body(i):
                for k in range(2):
                    u = 2 * i + k
                    wait(act, x_turned, DH * u + 1)
                    wait(act, value_made[k], CT * i)
                    act.activation(xT[:, k, 0, :], turn_bank[0][:], ACT.Copy).then_inc(xT_ready[0], 1)
                    for h in range(H):
                        wait(act, key_made, H * u + h + 1)
                        act.activation(kT[:, h, bass.ds(u * CN, CN)], key_bank[h % 2][:], ACT.Identity,
                                       bias=bk[:, h:h + 1]).then_inc(key_hi, 1)
            first_and_rest(act, CHUNKS // 2, body)

        @block.vector
        def _(dve):
            dve.wait_ge(weights_loaded, 16 * WEIGHT_LOADS)
            def body(i):
                for k in range(2):
                    u = 2 * i + k
                    wait(dve, x_turned, DH * u + 2)
                    wait(dve, value_made[k], CT * i)
                    dve.tensor_copy(xT[:, k, 1, :], turn_bank[1][:]).then_inc(xT_ready[1], 1)
                    for h in range(H):
                        wait(dve, key_hi, H * u + h + 1)
                        part = kT[HD:P, h, bass.ds(u * CN, CN)]
                        dve.scalar_tensor_tensor(out=part, in0=key_bank[h % 2][HD:P, :], scalar=bk[HD:P, h:h + 1],
                                                 in1=part.bitcast(F32), op0=ALU.add, op1=ALU.subtract)\
                           .then_inc(key_lo[h % 2], 1)
                    wait(dve, value_stored[k], 16 * H * i)
                    for t in range(CT):
                        wait(dve, value_made[k], CT * i + t + 1)
                        last = dve.tensor_tensor(v_out[:, k, t, :], value_bank[t % 2][:, 0:D], bv[:], ALU.add)
                        last.then_inc(value_out[t % 2], 1)
            first_and_rest(dve, CHUNKS // 2, body)


def layer0_attention(nc, x, adj, Wqkv, bqkv, Wout, bout, graph_bias, kT, v_heads, x1, x1_stored):
    CT = 2
    CN = CT * P
    CHUNKS = N // CN
    PIECE = 1024
    PIECES = N // PIECE
    STEP_PIECES = CT * PIECES
    GROUP = 2
    GROUPS = NT // GROUP
    BP = 512
    BPS = N // BP
    ON_ACT = list(range(1, 11))
    ON_DVE = [j for j in range(GROUPS) if j not in ON_ACT]
    FIRST_S = 1
    x_tiles, adj_tiles, x1_tiles, w_rows = tiles_of(x), tiles_of(adj), tiles_of(x1), tiles_of(Wqkv)
    with ExitStack() as ctx:
        sp = Space(nc, ctx, "at")
        probs = sp.sb("probs", [P, 2, CT, N])
        bias = sp.sb("bias", [P, CT, N])
        values = sp.sb("values", [P, 2, NT, HD])
        q = sp.sb("q", [P, H, 2, CN], F32R)
        masked = sp.sb("masked", [P, BP])
        pT = sp.sb("pT", [P, 2, GROUP * CN])
        xs = sp.sb("xs", [P, CT, D])
        xT = sp.sb("xT", [P, DH, CN])
        acc = sp.sb("acc", [P, CT, D])
        wq = sp.sb("wq", [P, DH, H, 2 * HD])
        wo = sp.sb("wo", [P, H, D])
        oT = sp.sb("oT", [P, CN])
        ident = sp.sb("ident", [P, P])
        bo = sp.sb("bo", [P, D])
        bq = sp.sb("bq", [P, H])
        gain = sp.sb("gain", [P, 1])
        maxima = sp.sb("maxima", [P, CT, PIECES])
        minus_max = sp.sb("minus_max", [P, 2, CT])
        sums = sp.sb("sums", [P, 2, CT, PIECES])
        sum_all = sp.sb("sum_all", [P, CT])
        inv_sum = sp.sb("inv_sum", [P, 2, CT])
        ln = LayerNorm(sp, CT)
        score_bank = [sp.ps(f"score{i}", (P, PIECE)) for i in range(2)]
        turn_bank = [sp.ps(f"turn{i}") for i in range(2)]
        o_bank = sp.ps("o")
        mixed_bank = sp.ps("mixed")

        ident_made = sp.sem("ident_made")
        const_loaded = sp.sem("const_loaded")
        gain_ready = sp.sem("gain_ready")
        passed = sp.sem("passed")
        x_loaded = sp.sem("x_loaded")
        x_turned = sp.sem("x_turned")
        xT_ready = sp.sem("xT_ready")
        q_made, q_hi, q_lo = sp.sem("q_made"), sp.sem("q_hi"), sp.sem("q_lo")
        adj_loaded = [sp.sem(f"adj_loaded{t}") for t in range(CT)]
        masked_ready = sp.sem("masked_ready")
        bias_ready = [sp.sem(f"bias_ready{t}") for t in range(CT)]
        score_made = sp.sem("score_made")
        score_read = sp.sem("score_read")
        max_ready = sp.sem("max_ready")
        prob_ready = sp.sem("prob_ready")
        sum_ready = sp.sem("sum_ready")
        inv_ready = sp.sem("inv_ready")
        turned = sp.sem("turned")
        pT_act, pT_dve = sp.sem("pT_act"), sp.sem("pT_dve")
        value_loaded = [sp.sem(f"value_loaded{k}") for k in range(2)]
        aggregated = sp.sem("aggregated")
        oT_ready = sp.sem("oT_ready")
        projected = sp.sem("projected")
        acc_start = sp.sem("acc_start")
        acc_ready = sp.sem("acc_ready")
        block = ctx.enter_context(nc.Block())
        CONST_LOADS = 2 * DH + 2 + 2 * H + 1 + 1

        def wait_pT(eng, s, j):
            if j < 0:
                s, j = s - 1, j + GROUPS
            if isinstance(s, int) and s < 0:
                return
            if j in ON_ACT:
                eng.wait_ge(pT_act, len(ON_ACT) * s + ON_ACT.index(j) + 1)
            else:
                eng.wait_ge(pT_dve, len(ON_DVE) * s + ON_DVE.index(j) + 1)

        def chunks(eng, body):
            body(0, False)
            with eng.Fori(1, CHUNKS - 1) as c:
                body(c, False)
            body(CHUNKS - 1, True)

        @block.sync
        def _(sync):
            sync.dma_start(xs[:], x_tiles[:, 0:CT, :]).then_inc(x_loaded, 16)
            for half in range(DH):
                for copy in range(2):
                    sync.dma_start(wq[:, half, :, copy * HD:(copy + 1) * HD],
                                   w_rows[:, half, 0:D].rearrange("p (h e) -> p h e", h=H))\
                        .then_inc(const_loaded, 16)
            for copy in range(2):
                sync.dma_start(wo[copy * HD:(copy + 1) * HD, :, :], Wout.rearrange("(h e) d -> e h d", h=H))\
                    .then_inc(const_loaded, 16)
                for h in range(H):
                    sync.dma_start(bq[copy * HD:(copy + 1) * HD, h:h + 1],
                                   bqkv[h * HD:(h + 1) * HD].rearrange("(e o) -> e o", o=1)).then_inc(const_loaded, 16)
            sync.dma_start(bo[:], bout.rearrange("(a d) -> a d", a=1).to_broadcast([P, D])).then_inc(const_loaded, 16)
            sync.dma_start(gain[:], graph_bias.rearrange("a b c -> (a b) c").to_broadcast([P, 1]))\
                .then_inc(const_loaded, 16)
            for t in range(CT):
                sync.dma_start(bias[:, t:t + 1, :], adj_tiles[:, t:t + 1, :]).then_inc(adj_loaded[t], 16)
            sync.dma_start(values[:, 0, :, :], v_heads[0]).then_inc(value_loaded[0], 16)

            def body(c, last):
                for h in range(H):
                    s = H * c + h
                    if not (last and h == H - 1):
                        wait(sync, aggregated, GROUPS * s)
                        k = (h + 1) % 2
                        sync.dma_start(values[:, k, :, :], v_heads[(h + 1) % H]).then_inc(value_loaded[k], 16)
                    if h == 0 and not last:
                        sync.wait_ge(acc_start, CT * (c + 1))
                        sync.wait_ge(x_turned, c + 1)
                        sync.dma_start(xs[:], x_tiles[:, bass.ds((c + 1) * CT, CT), :]).then_inc(x_loaded, 16)
                    if h == H - 2 and not last:
                        for t in range(CT):
                            sync.wait_ge(score_read, STEP_PIECES * (s + 1) + PIECES * (t + 1))
                            sync.dma_start(bias[:, t:t + 1, :], adj_tiles[:, bass.ds((c + 1) * CT + t, 1), :])\
                                .then_inc(adj_loaded[t], 16)
            chunks(sync, body)
            sync.wait_ge(x1_stored, 16 * CHUNKS)

        @block.gpsimd
        def _(pool):
            make_identity(pool, ident, ident_made)
            ln.constants(pool)

            def finish(c):
                ln.power(pool, c)
                pool.wait_ge(ln.norm_done, CT * (c + 1))
                pool.dma_start(x1_tiles[:, bass.ds(c * CT, CT), :], acc[:]).then_inc(x1_stored, 16)
            finish(0)
            with pool.Fori(1, CHUNKS) as c:
                finish(c)

        @block.tensor
        def _(pe):
            pe.wait_ge(ident_made, 2)
            pe.wait_ge(const_loaded, 16 * CONST_LOADS)

            def turn_x(c):
                pe.wait_ge(x_loaded, 16 * (c + 1))
                for half in range(DH):
                    for t in range(CT):
                        last = pe.transpose(mixed_bank[:, half * CN + t * P:half * CN + (t + 1) * P],
                                            xs[:, t, half * P:(half + 1) * P], ident[:])
                last.then_inc(x_turned, 1)

            def make_q(c, h):
                if h == 0:
                    pe.wait_ge(xT_ready, c + 1)
                for half in range(DH):
                    last = pe.matmul(mixed_bank[:, 0:CN], wq[:, half, h, :], xT[:, half, :],
                                     start=half == 0, stop=half == DH - 1)
                last.then_inc(q_made, 1)

            def make_scores(s, c, h, piece):
                if piece == 0:
                    pe.wait_ge(q_lo, H * c + h + 1)
                t, col = piece // PIECES, piece % PIECES * PIECE
                wait(pe, score_read, STEP_PIECES * s + piece - 1)
                for bank in range(PIECE // BANK):
                    at = slice(bank * BANK, (bank + 1) * BANK)
                    for part in range(2):
                        last = pe.matmul(score_bank[piece % 2][:, at], q[:, h, part, t * P:(t + 1) * P],
                                         kT[:, h, col + bank * BANK:col + (bank + 1) * BANK],
                                         start=part == 0, stop=part == 1)
                last.then_inc(score_made, 1)

            def turn_probs(s, k, j):
                wait_pT(pe, s, j - 2)
                if j % (GROUPS // PIECES) == 0:
                    piece = j // (GROUPS // PIECES)
                    pe.wait_ge(prob_ready, STEP_PIECES * s + STEP_PIECES - PIECES + piece + 1)
                for a in range(GROUP):
                    m = GROUP * j + a
                    for t in range(CT):
                        last = pe.transpose(turn_bank[j % 2][:, a * CN + t * P:a * CN + (t + 1) * P],
                                            probs[:, k, t, m * P:(m + 1) * P], ident[:])
                last.then_inc(turned, 1)

            def aggregate(s, c, h, j):
                wait_pT(pe, s, j)
                if j == 0:
                    wait(pe, oT_ready, s)
                    pe.wait_ge(value_loaded[h % 2], 16 * (H // 2 * c + h // 2 + 1))
                for a in range(GROUP):
                    last = pe.matmul(o_bank[a * HD:(a + 1) * HD, 0:CN], values[:, h % 2, GROUP * j + a, :],
                                     pT[:, j % 2, a * CN:(a + 1) * CN], start=j == 0, stop=j == GROUPS - 1)
                last.then_inc(aggregated, 1)

            def project(s, h):
                pe.wait_ge(oT_ready, s + 1)
                for t in range(CT):
                    last = pe.matmul(mixed_bank[:, t * D:(t + 1) * D], oT[:, t * P:(t + 1) * P], wo[:, h, :],
                                     start=True, stop=True)
                last.then_inc(projected, 1)

            turn_x(0)
            for h in range(H):
                wait(pe, q_lo, h)
                make_q(0, h)
            for piece in range(STEP_PIECES):
                make_scores(0, 0, 0, piece)

            def body(c, last):
                for h in range(H):
                    s = H * c + h
                    before = (c, h - 1) if h else (c - 1, H - 1)
                    after = (c, h + 1) if h < H - 1 else (c + 1, 0)
                    has_before = not (isinstance(s, int) and s == 0)
                    has_after = not (last and h == H - 1)
                    for j in range(GROUPS):
                        if has_after and FIRST_S <= j < FIRST_S + STEP_PIECES:
                            make_scores(s + 1, *after, j - FIRST_S)
                        turn_probs(s, h % 2, j)
                        if j:
                            aggregate(s, c, h, j - 1)
                        elif has_before:
                            aggregate(s - 1, *before, GROUPS - 1)
                        if j == 3 and has_before:
                            if h == 0:
                                pe.wait_ge(q_lo, H * c + H)
                            elif h == 2 and not last:
                                pe.wait_ge(xT_ready, c + 2)
                            elif h == 3 and not last:
                                pe.wait_ge(q_lo, H * (c + 1) + H - 1)
                            elif isinstance(s, int) and s == 1:
                                pe.wait_ge(q_lo, H)
                            else:
                                wait(pe, acc_ready, s - 1)
                            project(s - 1, before[1])
                        if last:
                            continue
                        if h == 1 and j == 11:
                            pe.wait_ge(acc_ready, s)
                            turn_x(c + 1)
                        if h == 2 and j in (10, 12, 14):
                            head = (j - 10) // 2
                            if head:
                                pe.wait_ge(q_lo, H * (c + 1) + head)
                            else:
                                pe.wait_ge(acc_ready, s)
                            make_q(c + 1, head)
                        if h == 3 and j == 10:
                            pe.wait_ge(acc_ready, s)
                            make_q(c + 1, H - 1)
            chunks(pe, body)
            final = H * CHUNKS - 1
            aggregate(final, CHUNKS - 1, H - 1, GROUPS - 1)
            pe.wait_ge(acc_ready, final)
            project(final, H - 1)

        @block.scalar
        def _(act):
            act.wait_ge(const_loaded, 16 * CONST_LOADS)

            def keep_xT(c):
                act.wait_ge(x_turned, c + 1)
                wait(act, q_made, H * c)
                act.activation(xT[:].rearrange("p a n -> p (a n)"), mixed_bank[:], ACT.Copy).then_inc(xT_ready, 1)

            def keep_q(c, h):
                act.wait_ge(q_made, H * c + h + 1)
                wait(act, score_made, STEP_PIECES * (H * (c - 1) + h + 1))
                act.activation(q[:, h, 0, :], mixed_bank[:, 0:CN], ACT.Identity, bias=bq[:, h:h + 1]).then_inc(q_hi, 1)

            def exponentials(s, k, piece):
                t, pp = piece // PIECES, piece % PIECES
                if pp == 0:
                    act.wait_ge(max_ready, CT * s + t + 1)
                if piece == 0:
                    wait(act, inv_ready, s - 1)
                part = probs[:, k, t, pp * PIECE:(pp + 1) * PIECE]
                act.activation(part, part, ACT.Exp, bias=minus_max[:, k, t:t + 1], scale=1.0,
                               accum_out=sums[:, k, t, pp:pp + 1]).then_inc(prob_ready, 1)

            def keep_oT(s):
                act.wait_ge(aggregated, GROUPS * (s + 1))
                wait(act, projected, s)
                act.activation(oT[:], o_bank[:, 0:CN], ACT.Copy).then_inc(oT_ready, 1)

            keep_xT(0)
            for h in range(H):
                keep_q(0, h)
            for piece in range(STEP_PIECES):
                exponentials(0, 0, piece)

            def body(c, last):
                for h in range(H):
                    s = H * c + h
                    has_before = not (isinstance(s, int) and s == 0)
                    has_after = not (last and h == H - 1)
                    for j in range(GROUPS):
                        if j == 1 and has_before:
                            keep_oT(s - 1)
                        if j in ON_ACT:
                            act.wait_ge(turned, GROUPS * s + j + 1)
                            wait(act, aggregated, GROUPS * s + j - 1)
                            act.activation(pT[:, j % 2, :], turn_bank[j % 2][:], ACT.Copy).then_inc(pT_act, 1)
                        if has_after and 6 <= j < 6 + STEP_PIECES:
                            exponentials(s + 1, (h + 1) % 2, j - 6)
                        if last:
                            continue
                        if h == 1 and j == 12:
                            keep_xT(c + 1)
                        if h == 2 and j in (11, 13, 15):
                            keep_q(c + 1, (j - 11) // 2)
                        if h == 3 and j == 11:
                            keep_q(c + 1, H - 1)
            chunks(act, body)
            keep_oT(H * CHUNKS - 1)

        @block.vector
        def _(dve):
            dve.wait_ge(const_loaded, 16 * CONST_LOADS)
            dve.tensor_scalar(gain[:], gain[:], 1.0 / SCALE, None, ALU.mult).then_inc(gain_ready, 1)
            dve.wait_ge(gain_ready, 1)

            def make_bias(c, t, b):
                if b == 0:
                    dve.wait_ge(adj_loaded[t], 16 * (c + 1))
                part = bias[:, t, b * BP:(b + 1) * BP]
                if b:
                    dve.wait_ge(bias_ready[t], BPS * c + b)
                else:
                    wait(dve, bias_ready[1 - t], BPS * (c + t))
                dve.tensor_scalar(masked[:], part, 0.0, MASKED / SCALE, ALU.is_equal, ALU.mult)\
                   .then_inc(masked_ready, 1)
                dve.wait_ge(masked_ready, CT * BPS * c + BPS * t + b + 1)
                dve.scalar_tensor_tensor(out=part, in0=part, scalar=gain[:, 0:1], in1=masked[:],
                                         op0=ALU.mult, op1=ALU.add).then_inc(bias_ready[t], 1)

            def finish_q(c, h):
                dve.wait_ge(q_hi, H * c + h + 1)
                dve.scalar_tensor_tensor(out=q[:, h, 1, :], in0=mixed_bank[:, 0:CN], scalar=bq[:, h:h + 1],
                                         in1=q[:, h, 0, :].bitcast(F32), op0=ALU.add, op1=ALU.subtract)\
                   .then_inc(q_lo, 1)

            def read_scores(s, c, h, k, piece):
                t, pp = piece // PIECES, piece % PIECES
                if pp == 0:
                    wait(dve, max_ready, CT * (s - 1) + t + 1)
                if piece == 0:
                    wait(dve, turned, GROUPS * (s - 1))
                if h == 0:
                    dve.wait_ge(bias_ready[t], BPS * c + (pp + 1) * PIECE // BP)
                at = slice(pp * PIECE, (pp + 1) * PIECE)
                wait_apart(dve, score_made, STEP_PIECES * s + piece + 1, passed)
                dve.tensor_tensor_reduce(out=probs[:, k, t, at], in0=score_bank[piece % 2][:], in1=bias[:, t, at],
                                         scale=SCALE, scalar=LOWEST, op0=ALU.add, op1=ALU.max,
                                         accum_out=maxima[:, t, pp:pp + 1]).then_inc(score_read, 1)
                if pp == PIECES - 1:
                    dve.wait_ge(score_read, STEP_PIECES * s + piece + 1)
                    dve.tensor_reduce(minus_max[:, k, t:t + 1], maxima[:, t, :], AX.X, ALU.max, negate=True)\
                       .then_inc(max_ready, 1)

            def invert_sums(s, k):
                dve.wait_ge(prob_ready, STEP_PIECES * (s + 1))
                wait(dve, inv_ready, s)
                wait(dve, acc_ready, s - 1)
                dve.tensor_reduce(sum_all[:], sums[:, k, :, :], AX.X, ALU.add).then_inc(sum_ready, 1)
                dve.wait_ge(sum_ready, s + 1)
                dve.reciprocal(inv_sum[:, k, :], sum_all[:]).then_inc(inv_ready, 1)

            def start_acc(c):
                wait(dve, x1_stored, 16 * c)
                dve.wait_ge(x_loaded, 16 * (c + 1))
                for t in range(CT):
                    dve.tensor_tensor(acc[:, t, :], xs[:, t, :], bo[:], ALU.add).then_inc(acc_start, 1)

            def add_step(s, h, k, c):
                dve.wait_ge(projected, s + 1)
                dve.wait_ge(inv_ready, s + 1)
                if h == 0:
                    dve.wait_ge(acc_start, CT * (c + 1))
                else:
                    dve.wait_ge(acc_ready, s)
                for t in range(CT):
                    last = dve.scalar_tensor_tensor(out=acc[:, t, :], in0=mixed_bank[:, t * D:(t + 1) * D],
                                                    scalar=inv_sum[:, k, t:t + 1], in1=acc[:, t, :],
                                                    op0=ALU.mult, op1=ALU.add)
                last.then_inc(acc_ready, 1)

            for t in range(CT):
                for b in range(BPS):
                    make_bias(0, t, b)
            for h in range(H):
                finish_q(0, h)
            for piece in range(STEP_PIECES):
                read_scores(0, 0, 0, 0, piece)

            def body(c, last):
                for h in range(H):
                    s = H * c + h
                    before = (c, h - 1) if h else (c - 1, H - 1)
                    after = (c, h + 1) if h < H - 1 else (c + 1, 0)
                    has_before = not (isinstance(s, int) and s == 0)
                    has_after = not (last and h == H - 1)
                    for j in range(GROUPS):
                        if j in ON_DVE:
                            dve.wait_ge(turned, GROUPS * s + j + 1)
                            wait(dve, aggregated, GROUPS * s + j - 1)
                            dve.tensor_copy(pT[:, j % 2, :], turn_bank[j % 2][:]).then_inc(pT_dve, 1)
                        if has_after and FIRST_S <= j < FIRST_S + STEP_PIECES:
                            read_scores(s + 1, *after, (h + 1) % 2, j - FIRST_S)
                        if j == 5 and has_before:
                            add_step(s - 1, before[1], before[1] % 2, before[0])
                            if h == 0:
                                dve.wait_ge(acc_ready, s)
                                ln.statistics(dve, acc, c - 1)
                        if j == 9:
                            invert_sums(s, h % 2)
                        if h == 0 and j == 9 and has_before:
                            ln.normalise(dve, acc, c - 1)
                        if h == 0 and j == 14:
                            start_acc(c)
                        if last:
                            continue
                        if h == 2 and j >= GROUPS - BPS // 2:
                            for b in range(2):
                                make_bias(c + 1, 0, 2 * (j - GROUPS + BPS // 2) + b)
                        if h == 3 and FIRST_S <= j < FIRST_S + BPS // 2:
                            for b in range(2):
                                make_bias(c + 1, 1, 2 * (j - FIRST_S) + b)
                        if h == 2 and j in (11, 13, 15):
                            finish_q(c + 1, (j - 11) // 2)
                        if h == 3 and j == 11:
                            finish_q(c + 1, H - 1)
            chunks(dve, body)
            final = H * CHUNKS - 1
            add_step(final, H - 1, (H - 1) % 2, CHUNKS - 1)
            dve.wait_ge(acc_ready, final + 1)
            ln.statistics(dve, acc, CHUNKS - 1)
            ln.normalise(dve, acc, CHUNKS - 1)
    return sp.semaphores


def layer1_values(nc, x1, W, a, wh_hi, wh_lo, minus_src, dst_row):
    CT = 4
    CN = CT * P
    CHUNKS = N // CN
    x_tiles, w_rows = tiles_of(x1), tiles_of(W)
    with ExitStack() as ctx:
        sp = Space(nc, ctx, "wh")
        ident = sp.sb("ident", [P, P])
        w = sp.sb("w", [P, DH, D])
        a_rows = sp.sb("a_rows", [P, 2, D])
        xs = sp.sb("xs", [P, 2, CT, D])
        xT = sp.sb("xT", [P, 2, DH, CN])
        product = sp.sb("product", [P, CT, 2, D])
        src = sp.sb("src", [P, CT])
        dst = sp.sb("dst", [P, CT])
        dst_wide = sp.sb("dst_wide", [P, CT, P])
        turn_bank = [sp.ps(f"turn{i}") for i in range(DH)]
        wh_bank = [sp.ps(f"wh{i}") for i in range(2)]
        row_bank = sp.ps("row")
        ident_made = sp.sem("ident_made")
        weights_loaded = sp.sem("weights_loaded")
        x_loaded = [sp.sem(f"x_loaded{k}") for k in range(2)]
        x_turned = sp.sem("x_turned")
        xT_ready = [sp.sem(f"xT_ready{i}") for i in range(DH)]
        wh_made = [sp.sem(f"wh_made{k}") for k in range(2)]
        hi_ready = sp.sem("hi_ready")
        wh_read = [sp.sem(f"wh_read{b}") for b in range(2)]
        src_ready, dst_ready = sp.sem("src_ready"), sp.sem("dst_ready")
        minus_ready = sp.sem("minus_ready")
        wide_ready = sp.sem("wide_ready")
        row_made, row_ready = sp.sem("row_made"), sp.sem("row_ready")
        block = ctx.enter_context(nc.Block())

        @block.sync
        def _(sync):
            for k in range(2):
                sync.dma_start(xs[:, k, :, :], x_tiles[:, k * CT:(k + 1) * CT, :]).then_inc(x_loaded[k], 16)
            sync.dma_start(w[:], w_rows).then_inc(weights_loaded, 16)
            for part in range(2):
                sync.dma_start(a_rows[:, part, :], a[part * D:(part + 1) * D].rearrange("(o d) -> o d", o=1)
                               .to_broadcast([P, D])).then_inc(weights_loaded, 16)
            with sync.Fori(0, CHUNKS // 2 - 1) as i:
                for k in range(2):
                    u = 2 * i + k
                    sync.wait_ge(x_turned, DH * (u + 1))
                    sync.dma_start(xs[:, k, :, :], x_tiles[:, bass.ds((u + 2) * CT, CT), :])\
                        .then_inc(x_loaded[k], 16)

        @block.gpsimd
        def _(pool):
            make_identity(pool, ident, ident_made)

        @block.tensor
        def _(pe):
            pe.wait_ge(ident_made, 2)
            pe.wait_ge(weights_loaded, 48)
            def body(i):
                for k in range(2):
                    u = 2 * i + k
                    wait(pe, x_loaded[k], 16 * (i + 1))
                    for half in range(DH):
                        wait(pe, xT_ready[half], u)
                        for t in range(CT):
                            last = pe.transpose(turn_bank[half][:, t * P:(t + 1) * P],
                                                xs[:, k, t, half * P:(half + 1) * P], ident[:])
                        last.then_inc(x_turned, 1)
                    for half in range(DH):
                        wait(pe, xT_ready[half], u + 1)
                    for t in range(CT):
                        b = t % 2
                        wait(pe, wh_read[b], CT // 2 * u + t // 2)
                        for half in range(DH):
                            last = pe.matmul(wh_bank[b][:, 0:D], xT[:, k, half, t * P:(t + 1) * P],
                                             w[:, half, :], start=half == 0, stop=half == DH - 1)
                        last.then_inc(wh_made[k], 1)
                    wait(pe, wide_ready, CT * (u + 1))
                    wait(pe, row_ready, u)
                    for t in range(CT):
                        last = pe.matmul(row_bank[:, t * P:(t + 1) * P], dst_wide[:, t, :], ident[:],
                                         start=True, stop=True)
                    last.then_inc(row_made, 1)
            first_and_rest(pe, CHUNKS // 2, body)

        @block.scalar
        def _(act):
            def body(i):
                for k in range(2):
                    u = 2 * i + k
                    wait(act, x_turned, DH * u + 1)
                    wait(act, wh_made[k], CT * i)
                    act.activation(xT[:, k, 0, :], turn_bank[0][:], ACT.Copy).then_inc(xT_ready[0], 1)
                    for t in range(CT):
                        wait(act, wh_made[k], CT * i + t + 1)
                        act.activation(wh_hi[:, bass.ds((u * CT + t) * D, D)], wh_bank[t % 2][:, 0:D], ACT.Copy)\
                           .then_inc(hi_ready, 1)
                    wait(act, row_made, u + 1)
                    act.activation(dst_row[:, bass.ds(u * CN, CN)], row_bank[:], ACT.Copy).then_inc(row_ready, 1)
            first_and_rest(act, CHUNKS // 2, body)

        @block.vector
        def _(dve):
            dve.wait_ge(weights_loaded, 48)
            def body(i):
                for k in range(2):
                    u = 2 * i + k
                    wait(dve, x_turned, DH * u + 2)
                    wait(dve, wh_made[k], CT * i)
                    dve.tensor_copy(xT[:, k, 1, :], turn_bank[1][:]).then_inc(xT_ready[1], 1)
                    wait(dve, minus_ready, u)
                    wait(dve, wide_ready, CT * u)
                    for t in range(CT):
                        wait(dve, hi_ready, CT * u + t + 1)
                        bank = wh_bank[t % 2][:, 0:D]
                        dve.tensor_tensor_reduce(out=product[:, t, 0, :], in0=bank, in1=a_rows[:, 0, :], scale=1.0,
                                                 scalar=0.0, op0=ALU.mult, op1=ALU.add, accum_out=src[:, t:t + 1])\
                           .then_inc(src_ready, 1)
                        dve.tensor_tensor_reduce(out=product[:, t, 1, :], in0=bank, in1=a_rows[:, 1, :], scale=1.0,
                                                 scalar=0.0, op0=ALU.mult, op1=ALU.add, accum_out=dst[:, t:t + 1])\
                           .then_inc(dst_ready, 1)
                        at = bass.ds((u * CT + t) * D, D)
                        dve.tensor_tensor(wh_lo[:, at], bank, wh_hi[:, at].bitcast(F32), ALU.subtract)\
                           .then_inc(wh_read[t % 2], 1)
                    wait(dve, src_ready, CT * (u + 1))
                    dve.tensor_scalar(minus_src[:, bass.ds(u * CT, CT)], src[:], -1.0, None, ALU.mult)\
                       .then_inc(minus_ready, 1)
                    wait(dve, dst_ready, CT * (u + 1))
                    wait(dve, row_made, u)
                    for t in range(CT):
                        dve.tensor_copy(dst_wide[:, t, :], dst[:, t:t + 1].to_broadcast([P, P])).then_inc(wide_ready, 1)
            first_and_rest(dve, CHUNKS // 2, body)


class Aggregator:

    CT = 4
    CN = CT * P
    CHUNKS = N // CN
    STEPS = NT
    RING = 4
    LAG = 3

    def __init__(self, space, values_hi, values_lo, ident):
        self.values_hi, self.values_lo, self.ident = values_hi, values_lo, ident
        self.hi = space.sb("hi", [P, self.RING, self.CN], F32R)
        self.lo = space.sb("lo", [P, self.RING, self.CN], F32R)
        self.outT = space.sb("outT", [P, DH, self.CN])
        self.turn_bank = [space.ps(f"turn{i}") for i in range(self.RING)]
        self.out_bank = [space.ps(f"out{i}") for i in range(DH)]
        self.turned = space.sem("turned")
        self.hi_ready = space.sem("hi_ready")
        self.lo_ready = space.sem("lo_ready")
        self.multiplied = space.sem("multiplied")
        self.outT_ready = [space.sem(f"outT_ready{i}") for i in range(DH)]

    def turn(self, pe, c, step, weights):
        g, slot = self.STEPS * c + step, step % self.RING
        wait(pe, self.lo_ready, g - self.RING + 1)
        for t, block in enumerate(weights):
            last = pe.transpose(self.turn_bank[slot][:, t * P:(t + 1) * P], block, self.ident[:])
        last.then_inc(self.turned, 1)

    def multiply(self, pe, c, step, m):
        slot = step % self.RING
        pe.wait_ge(self.lo_ready, self.STEPS * c + step + 1)
        for half in range(DH):
            if step == 0:
                wait(pe, self.outT_ready[half], c)
            at = slice(m * D + half * P, m * D + (half + 1) * P)
            first, final = step == 0, step == self.STEPS - 1
            pe.matmul(self.out_bank[half][:], self.values_hi[:, at], self.hi[:, slot, :], start=first, stop=False)
            pe.matmul(self.out_bank[half][:], self.values_hi[:, at], self.lo[:, slot, :], start=False, stop=False)
            last = pe.matmul(self.out_bank[half][:], self.values_lo[:, at], self.hi[:, slot, :],
                             start=False, stop=final)
        last.then_inc(self.multiplied, 1)

    def read_hi(self, act, c, step):
        g, slot = self.STEPS * c + step, step % self.RING
        act.wait_ge(self.turned, g + 1)
        wait(act, self.multiplied, g - self.RING + 1)
        act.activation(self.hi[:, slot, :], self.turn_bank[slot][:], ACT.Copy).then_inc(self.hi_ready, 1)

    def read_lo(self, dve, c, step):
        g, slot = self.STEPS * c + step, step % self.RING
        dve.wait_ge(self.hi_ready, g + 1)
        dve.tensor_tensor(self.lo[:, slot, :], self.turn_bank[slot][:], self.hi[:, slot, :].bitcast(F32),
                          ALU.subtract).then_inc(self.lo_ready, 1)

    def keep_out(self, eng, copy, half, c, out_used):
        eng.wait_ge(self.multiplied, self.STEPS * (c + 1))
        wait(eng, out_used, c)
        copy(self.outT[:, half, :], self.out_bank[half][:]).then_inc(self.outT_ready[half], 1)


def paired_chunks(eng, body):
    pairs = Aggregator.CHUNKS // 2
    body(0, False)
    with eng.Fori(1, pairs - 1) as i:
        body(i, False)
    body(pairs - 1, True)


def layer1_attention(nc, x1, adj, wh_hi, wh_lo, minus_src, dst_row, inv_deg2, inv_deg3, x2, x2_stored):
    CT, CN, CHUNKS, STEPS, LAG = Aggregator.CT, Aggregator.CN, Aggregator.CHUNKS, Aggregator.STEPS, Aggregator.LAG
    UNITS = 4
    UC = N // UNITS
    US = UC // P
    ITEMS = UNITS * CT
    SLOTS = 6
    FIRST_SLOT = (0, 2)
    TURN_SLOTS = ((2, 3, 0, 1), (2, 3, 4, 5))
    LOAD_SLOTS = ((0, 1, 2, 3), (4, 5, 2, 3))
    adj_tiles, x1_tiles, x2_tiles = tiles_of(adj), tiles_of(x1), tiles_of(x2)
    with ExitStack() as ctx:
        sp = Space(nc, ctx, "ga")
        unit = sp.sb("unit", [P, SLOTS, CT, UC])
        ident = sp.sb("ident", [P, P])
        off_diag = sp.sb("off_diag", [P, 2 * UNITS - 1, P])
        y = sp.sb("y", [P, CT, D])
        minus_s = sp.sb("minus_s", [P, CT])
        row_part = sp.sb("row_part", [P, CT, UNITS])
        row_sum = sp.sb("row_sum", [P, CT])
        no_row = sp.sb("no_row", [P, CT])
        row_safe = sp.sb("row_safe", [P, CT])
        inv_safe = sp.sb("inv_safe", [P, CT])
        max_part = sp.sb("max_part", [P, CT, UNITS])
        max_dst = sp.sb("max_dst", [P, CT])
        max_sum = sp.sb("max_sum", [P, CT])
        max_leaky = sp.sb("max_leaky", [P, CT])
        shift = sp.sb("shift", [P, CT])
        sum_part = sp.sb("sum_part", [P, CT, UNITS])
        sum_all = sp.sb("sum_all", [P, CT])
        inv_sum = sp.sb("inv_sum", [P, CT])
        ag = Aggregator(sp, wh_hi, wh_lo, ident)
        ln = LayerNorm(sp, CT)
        back_bank = [sp.ps(f"back{i}") for i in range(2)]

        off_made = sp.sem("off_made")
        ident_made = sp.sem("ident_made")
        adj_loaded = [sp.sem(f"adj_loaded{i}") for i in range(SLOTS)]
        row_added = sp.sem("row_added")
        row_summed = sp.sem("row_summed")
        row_steps = sp.sem("row_steps")
        degree_power = sp.sem("degree_power")
        degree_done = sp.sem("degree_done")
        masked_dve, masked_pool = sp.sem("masked_dve"), sp.sem("masked_pool")
        passed_sync = sp.sem("passed_sync")
        passed_dve, passed_pool = sp.sem("passed_dve"), sp.sem("passed_pool")
        edges_dve, edges_pool = sp.sem("edges_dve"), sp.sem("edges_pool")
        minus_s_ready = sp.sem("minus_s_ready")
        max_read = sp.sem("max_read")
        max_steps = sp.sem("max_steps")
        shift_ready = sp.sem("shift_ready")
        logit_ready = sp.sem("logit_ready")
        weight_ready = sp.sem("weight_ready")
        sum_ready, inv_ready = sp.sem("sum_ready"), sp.sem("inv_ready")
        y_loaded = sp.sem("y_loaded")
        out_back = sp.sem("out_back")
        y_ready = sp.sem("y_ready")
        block = ctx.enter_context(nc.Block())

        POOL_ITEMS = [(n, t) for n in range(UNITS - 1) for t in (2, 3)]
        DVE_ITEMS = [(n, t) for n in range(UNITS) for t in range(CT) if (n, t) not in POOL_ITEMS]

        def quarter(k, slot):
            return slot - FIRST_SLOT[k]

        def load_times(k):
            return {s: (lambda i, k=k, s=s: 16 * (2 * i + k + 1) if s in (2, 3) else 16 * (i + 1)) for s in LOAD_SLOTS[k]}

        def following(i, k):
            return (i, 1) if k == 0 else (i + 1, 0)

        def mask(eng, c, i, k, n, t, masked, edges, passed, items):
            slot = LOAD_SLOTS[k][n]
            q = quarter(k, slot)
            at = items.index((n, t))
            wait_apart(eng, row_added, ITEMS * c + CT * n + t + 1, passed)
            eng.tensor_scalar(unit[:, slot, t, :], unit[:, slot, t, :], 0.0, NO_EDGE, ALU.is_le, ALU.mult)\
               .then_inc(masked, 1)
            wait_apart(eng, masked, len(items) * c + at + 1, passed)
            corner = k * CN + t * P
            part = unit[:, slot, t, corner:corner + P]
            eng.tensor_tensor(part, part, off_diag[:, bass.ds(q - i + UNITS - 1, 1), :].rearrange("p o m -> p (o m)"),
                              ALU.mult).then_inc(edges, 1)

        @block.sync
        def _(sync):
            def load(i, k, n):
                c = 2 * i + k
                slot = LOAD_SLOTS[k][n]
                if slot in (2, 3):
                    wait_apart(sync, ag.turned, STEPS * (c - 1) + US * (slot - 1), passed_sync)
                else:
                    wait_apart(sync, ag.turned, STEPS * (c - 1), passed_sync)
                q = quarter(k, slot)
                sync.dma_start(unit[:, slot, :, :], adj_tiles[:, bass.ds(c * CT, CT), q * UC:(q + 1) * UC])\
                    .then_inc(adj_loaded[slot], 16)

            for n in range(UNITS):
                load(0, 0, n)

            def body(i, last):
                for k in range(2):
                    c = 2 * i + k
                    nxt = following(i, k)
                    more = not (last and k == 1)
                    if more:
                        for n in range(UNITS - 1):
                            load(*nxt, n)
                    wait(sync, x2_stored, 16 * c)
                    sync.dma_start(y[:], x1_tiles[:, bass.ds(c * CT, CT), :]).then_inc(y_loaded, 16)
                    if more:
                        load(*nxt, UNITS - 1)
            paired_chunks(sync, body)
            sync.wait_ge(x2_stored, 16 * CHUNKS)

        @block.gpsimd
        def _(pool):
            make_identity(pool, ident, ident_made)
            pool.memset(off_diag[:], 1.0).then_inc(off_made, 1)
            ln.constants(pool)
            pool.wait_ge(off_made, 1)
            pool.wait_ge(ident_made, 2)
            pool.tensor_scalar(off_diag[:, UNITS - 1, :], ident[:], -1.0, 1.0, ALU.mult, ALU.add).then_inc(off_made, 1)
            pool.wait_ge(off_made, 2)
            pool.wait_ge(ln.half_made, 1)

            def degrees(c):
                pool.wait_ge(row_steps, 2 * c + 2)
                pool.tensor_tensor(inv_safe[:], row_safe[:], ln.minus_half[:], ALU.pow).then_inc(degree_power, 1)
                pool.tensor_tensor(inv_deg3[:, bass.ds(c * CT, CT)], row_sum[:], ln.minus_half[:], ALU.pow)\
                    .then_inc(degree_power, 1)
                wait_apart(pool, degree_power, 2 * c + 2, passed_pool)
                pool.tensor_tensor(inv_deg2[:, bass.ds(c * CT, CT)], inv_safe[:], no_row[:], ALU.subtract)\
                    .then_inc(degree_done, 1)

            def masks(i, k, n):
                c = 2 * i + k
                for t in (2, 3):
                    mask(pool, c, i, k, n, t, masked_pool, edges_pool, passed_pool, POOL_ITEMS)

            def finish(c):
                ln.power(pool, c)
                pool.wait_ge(ln.norm_done, CT * (c + 1))
                pool.dma_start(x2_tiles[:, bass.ds(c * CT, CT), :], y[:]).then_inc(x2_stored, 16)

            for n in range(UNITS - 1):
                masks(0, 0, n)
            degrees(0)

            def body(i, last):
                for k in range(2):
                    c = 2 * i + k
                    if not (isinstance(c, int) and c == 0):
                        finish(c - 1)
                    if not (last and k == 1):
                        for n in range(UNITS - 1):
                            masks(*following(i, k), n)
                        degrees(c + 1)
            paired_chunks(pool, body)
            finish(CHUNKS - 1)

        @block.tensor
        def _(pe):
            pe.wait_ge(ident_made, 2)

            def column_tile(k, step):
                return quarter(k, TURN_SLOTS[k][step // US]) * US + step % US

            def back(c):
                for half in range(DH):
                    pe.wait_ge(ag.outT_ready[half], c + 1)
                wait(pe, y_ready, c)
                for t in range(CT):
                    for half in range(DH):
                        at = t % 2 * D + half * P
                        last = pe.transpose(back_bank[t // 2][:, at:at + P], ag.outT[:, half, t * P:(t + 1) * P],
                                            ident[:])
                last.then_inc(out_back, 1)

            def body(i, last):
                for k in range(2):
                    c = 2 * i + k
                    has_before = not (isinstance(c, int) and c == 0)
                    for step in range(STEPS):
                        n, col = step // US, step % US * P
                        slot = TURN_SLOTS[k][n]
                        if step % US == 0:
                            pe.wait_ge(weight_ready, ITEMS * c + CT * (n + 1))
                        ag.turn(pe, c, step, [unit[:, slot, t, col:col + P] for t in range(CT)])
                        if step >= LAG:
                            ag.multiply(pe, c, step - LAG, column_tile(k, step - LAG))
                        elif has_before:
                            ag.multiply(pe, c - 1, STEPS + step - LAG, column_tile(1 - k, STEPS + step - LAG))
                        if step == 6 and has_before:
                            back(c - 1)
            paired_chunks(pe, body)
            for step in range(STEPS - LAG, STEPS):
                ag.multiply(pe, CHUNKS - 1, step, column_tile(1, step))
            back(CHUNKS - 1)

        @block.scalar
        def _(act):
            def add_rows(i, k, n, t):
                c = 2 * i + k
                slot = LOAD_SLOTS[k][n]
                if t == 0:
                    act.wait_ge(adj_loaded[slot], load_times(k)[slot](i))
                if n == 0 and t == 0:
                    wait(act, row_summed, c)
                part = unit[:, slot, t, :]
                act.activation(part, part, ACT.Copy, accum_out=row_part[:, t, n:n + 1]).then_inc(row_added, 1)

            def exponentials(i, k, n, t):
                c = 2 * i + k
                if n == 0 and t == 0:
                    act.wait_ge(shift_ready, c + 1)
                    wait(act, inv_ready, c)
                act.wait_ge(logit_ready, ITEMS * c + CT * n + t + 1)
                part = unit[:, TURN_SLOTS[k][n], t, :]
                act.activation(part, part, ACT.Exp, bias=shift[:, t:t + 1], scale=1.0 - SLOPE,
                               accum_out=sum_part[:, t, n:n + 1]).then_inc(weight_ready, 1)

            def copy(out, in_):
                return act.activation(out, in_, ACT.Copy)

            for n in range(UNITS):
                for t in range(CT):
                    add_rows(0, 0, n, t)
            for t in range(CT):
                exponentials(0, 0, 0, t)

            def body(i, last):
                for k in range(2):
                    c = 2 * i + k
                    more = not (last and k == 1)
                    has_before = not (isinstance(c, int) and c == 0)
                    for step in range(STEPS):
                        ag.read_hi(act, c, step)
                        if step == 2 and has_before:
                            ag.keep_out(act, copy, 0, c - 1, out_back)
                        if 1 <= step <= 6:
                            for t in range(2):
                                item = 2 * (step - 1) + t
                                exponentials(i, k, 1 + item // CT, item % CT)
                        for n, start in enumerate((8, 12, 16, 24)):
                            if more and step in (start, start + 1):
                                for t in range(2):
                                    add_rows(*following(i, k), n, 2 * (step - start) + t)
                        if more and step == STEPS - 1:
                            for t in range(CT):
                                exponentials(*following(i, k), 0, t)
            paired_chunks(act, body)
            ag.keep_out(act, copy, 0, CHUNKS - 1, out_back)

        @block.vector
        def _(dve):
            dve.wait_ge(off_made, 2)

            def start_rows(c):
                wait(dve, logit_ready, ITEMS * c)
                dve.tensor_copy(minus_s[:], minus_src[:, bass.ds(c * CT, CT)]).then_inc(minus_s_ready, 1)

            def masks(i, k, n, t):
                mask(dve, 2 * i + k, i, k, n, t, masked_dve, edges_dve, passed_dve, DVE_ITEMS)

            def read_max(i, k, n, t):
                c = 2 * i + k
                slot = LOAD_SLOTS[k][n]
                q = quarter(k, slot)
                if (n, t) in POOL_ITEMS:
                    wait_apart(dve, edges_pool, len(POOL_ITEMS) * c + POOL_ITEMS.index((n, t)) + 1, passed_dve)
                else:
                    wait_apart(dve, edges_dve, len(DVE_ITEMS) * c + DVE_ITEMS.index((n, t)) + 1, passed_dve)
                part = unit[:, slot, t, :]
                dve.tensor_tensor_reduce(out=part, in0=dst_row[:, q * UC:(q + 1) * UC], in1=part, scale=0.25,
                                         scalar=2 * NO_EDGE, op0=ALU.add, op1=ALU.max,
                                         accum_out=max_part[:, t, n:n + 1]).then_inc(max_read, 1)

            def make_shift(c):
                dve.wait_ge(max_read, ITEMS * (c + 1))
                dve.tensor_reduce(max_dst[:], max_part[:], AX.X, ALU.max).then_inc(max_steps, 1)
                dve.wait_ge(max_steps, 3 * c + 1)
                dve.wait_ge(minus_s_ready, c + 1)
                dve.scalar_tensor_tensor(out=max_sum[:], in0=max_dst[:], scalar=4.0, in1=minus_s[:],
                                         op0=ALU.mult, op1=ALU.subtract).then_inc(max_steps, 1)
                dve.wait_ge(max_steps, 3 * c + 2)
                dve.scalar_tensor_tensor(out=max_leaky[:], in0=max_sum[:], scalar=SLOPE, in1=max_sum[:],
                                         op0=ALU.mult, op1=ALU.max).then_inc(max_steps, 1)
                dve.wait_ge(max_steps, 3 * c + 3)
                dve.scalar_tensor_tensor(out=shift[:], in0=minus_s[:], scalar=-1.0, in1=max_leaky[:],
                                         op0=ALU.mult, op1=ALU.subtract).then_inc(shift_ready, 1)

            def logits(i, k, n, t):
                slot = TURN_SLOTS[k][n]
                q = quarter(k, slot)
                part = unit[:, slot, t, :]
                dve.scalar_tensor_tensor(out=part, in0=dst_row[:, q * UC:(q + 1) * UC], scalar=minus_s[:, t:t + 1],
                                         in1=part, op0=ALU.max, op1=ALU.add).then_inc(logit_ready, 1)

            def add_row_parts(c):
                dve.wait_ge(row_added, ITEMS * (c + 1))
                wait(dve, degree_done, c)
                wait(dve, degree_power, 2 * c)
                dve.tensor_reduce(row_sum[:], row_part[:], AX.X, ALU.add).then_inc(row_summed, 1)
                dve.wait_ge(row_summed, c + 1)
                dve.tensor_scalar(no_row[:], row_sum[:], 0.0, None, ALU.is_equal).then_inc(row_steps, 1)
                dve.wait_ge(row_steps, 2 * c + 1)
                dve.tensor_tensor(row_safe[:], row_sum[:], no_row[:], ALU.add).then_inc(row_steps, 1)

            def invert_sums(c):
                dve.wait_ge(weight_ready, ITEMS * (c + 1))
                wait(dve, y_ready, c)
                dve.tensor_reduce(sum_all[:], sum_part[:], AX.X, ALU.add).then_inc(sum_ready, 1)
                dve.wait_ge(sum_ready, c + 1)
                dve.reciprocal(inv_sum[:], sum_all[:]).then_inc(inv_ready, 1)

            def add_out(c):
                dve.wait_ge(out_back, c + 1)
                dve.wait_ge(y_loaded, 16 * (c + 1))
                dve.wait_ge(inv_ready, c + 1)
                for t in range(CT):
                    last = dve.scalar_tensor_tensor(out=y[:, t, :], in0=back_bank[t // 2][:, t % 2 * D:(t % 2 + 1) * D],
                                                    scalar=inv_sum[:, t:t + 1], in1=y[:, t, :],
                                                    op0=ALU.mult, op1=ALU.add)
                last.then_inc(y_ready, 1)
                dve.wait_ge(y_ready, c + 1)
                ln.statistics(dve, y, c)

            start_rows(0)
            for n, t in DVE_ITEMS:
                masks(0, 0, n, t)
            for n in range(UNITS):
                for t in range(CT):
                    read_max(0, 0, n, t)
            make_shift(0)
            add_row_parts(0)
            for t in range(CT):
                logits(0, 0, 0, t)

            MASKS = {9: [(0, 0), (0, 1)], 13: [(1, 0), (1, 1)], 18: [(2, 0), (2, 1)],
                     26: [(3, 0), (3, 1)], 27: [(3, 2), (3, 3)]}
            MAXIMA = {10: [(0, 0)], 11: [(0, 1)], 14: [(1, 0)], 15: [(1, 1)], 16: [(0, 2)], 17: [(0, 3)],
                      19: [(2, 0)], 20: [(2, 1)], 22: [(1, 2)], 23: [(1, 3)], 28: [(3, 0), (3, 1)],
                      29: [(3, 2), (3, 3)], 30: [(2, 2), (2, 3)]}

            def body(i, last):
                for k in range(2):
                    c = 2 * i + k
                    more = not (last and k == 1)
                    has_before = not (isinstance(c, int) and c == 0)
                    nxt = following(i, k)
                    for step in range(STEPS):
                        ag.read_lo(dve, c, step)
                        if step == 2 and has_before:
                            ag.keep_out(dve, dve.tensor_copy, 1, c - 1, out_back)
                        if step <= 5:
                            for t in range(2):
                                item = 2 * step + t
                                logits(i, k, 1 + item // CT, item % CT)
                        if step == 7 and has_before:
                            add_out(c - 1)
                        if step == 12:
                            if has_before:
                                ln.normalise(dve, y, c - 1)
                            invert_sums(c)
                        if not more:
                            continue
                        if step == 8:
                            start_rows(c + 1)
                        for n, t in MASKS.get(step, ()):
                            masks(*nxt, n, t)
                        for n, t in MAXIMA.get(step, ()):
                            read_max(*nxt, n, t)
                        if step == 27:
                            add_row_parts(c + 1)
                        if step == 30:
                            make_shift(c + 1)
                        if step == 31:
                            for t in range(CT):
                                logits(*nxt, 0, t)
            paired_chunks(dve, body)
            ag.keep_out(dve, dve.tensor_copy, 1, CHUNKS - 1, out_back)
            add_out(CHUNKS - 1)
            ln.normalise(dve, y, CHUNKS - 1)


def clear(nc, semaphores):
    with nc.Block() as block:
        @block.gpsimd
        def _(pool):
            for semaphore in semaphores:
                pool.sem_clear(semaphore)


def scaled_rows(nc, phase, x, inv_deg, rows_hi, rows_lo, cleared=None):
    CT = 4
    CHUNKS = NT // CT
    x_tiles = tiles_of(x)
    with ExitStack() as ctx:
        sp = Space(nc, ctx, phase, cleared)
        xs = sp.sb("xs", [P, 2, CT, D])
        scaled = sp.sb("scaled", [P, 2, CT * D])
        x_loaded = [sp.sem(f"x_loaded{k}") for k in range(2)]
        row_scaled = [sp.sem(f"row_scaled{k}") for k in range(2)]
        hi_ready = sp.sem("hi_ready")
        lo_ready = [sp.sem(f"lo_ready{k}") for k in range(2)]
        block = ctx.enter_context(nc.Block())

        @block.sync
        def _(sync):
            for u in range(CHUNKS):
                k = u % 2
                wait(sync, row_scaled[k], CT * (u // 2))
                sync.dma_start(xs[:, k, :, :], x_tiles[:, u * CT:(u + 1) * CT, :]).then_inc(x_loaded[k], 16)

        @block.scalar
        def _(act):
            for u in range(CHUNKS):
                k = u % 2
                act.wait_ge(row_scaled[k], CT * (u // 2 + 1))
                act.activation(rows_hi[:, u * CT * D:(u + 1) * CT * D], scaled[:, k, :], ACT.Copy).then_inc(hi_ready, 1)

        @block.vector
        def _(dve):
            def split(u):
                k = u % 2
                at = slice(u * CT * D, (u + 1) * CT * D)
                dve.wait_ge(hi_ready, u + 1)
                dve.tensor_tensor(rows_lo[:, at], scaled[:, k, :], rows_hi[:, at].bitcast(F32), ALU.subtract)\
                   .then_inc(lo_ready[k], 1)

            for u in range(CHUNKS):
                k = u % 2
                dve.wait_ge(x_loaded[k], 16 * (u // 2 + 1))
                wait(dve, lo_ready[k], u // 2)
                for t in range(CT):
                    dve.tensor_scalar(scaled[:, k, t * D:(t + 1) * D], xs[:, k, t, :],
                                      inv_deg[:, u * CT + t:u * CT + t + 1], None, ALU.mult).then_inc(row_scaled[k], 1)
                if u:
                    split(u - 1)
            split(CHUNKS - 1)


def graph_convolution(nc, phase, x, adj, W, b, inv_deg, rows_hi, rows_lo, x_next, next_stored, cleared=None):
    CT, CN, CHUNKS, STEPS, LAG = Aggregator.CT, Aggregator.CN, Aggregator.CHUNKS, Aggregator.STEPS, Aggregator.LAG
    UNITS = 4
    UC = N // UNITS
    US = UC // P
    adj_tiles, x_tiles, next_tiles, w_rows = tiles_of(adj), tiles_of(x), tiles_of(x_next), tiles_of(W)
    linear = b is not None
    with ExitStack() as ctx:
        sp = Space(nc, ctx, phase, cleared)
        unit = sp.sb("unit", [P, UNITS, CT, UC])
        ident = sp.sb("ident", [P, P])
        w_in = sp.sb("w_in", [P, DH, D])
        w = sp.sb("w", [P, DH, D]) if linear else w_in
        b_rows = sp.sb("b_rows", [P, D])
        y = sp.sb("y", [P, CT, D])
        relu = sp.sb("relu", [P, CT, D])
        scale = sp.sb("scale", [P, CT])
        ag = Aggregator(sp, rows_hi, rows_lo, ident)
        ln = LayerNorm(sp, CT)
        rows_bank = [sp.ps(f"rows{i}") for i in range(2)]

        ident_made = sp.sem("ident_made")
        const_loaded = sp.sem("const_loaded")
        w_turned = sp.sem("w_turned")
        w_ready = sp.sem("w_ready")
        adj_loaded = [sp.sem(f"adj_loaded{i}") for i in range(UNITS)]
        y_loaded = sp.sem("y_loaded")
        projected = sp.sem("projected")
        scale_ready = sp.sem("scale_ready")
        relu_ready = sp.sem("relu_ready")
        bias_added = sp.sem("bias_added")
        y_ready = sp.sem("y_ready")
        block = ctx.enter_context(nc.Block())
        CONST_LOADS = 1 + linear

        @block.sync
        def _(sync):
            def load(c, q):
                wait(sync, ag.turned, STEPS * (c - 1) + US * (q + 1))
                sync.dma_start(unit[:, q, :, :], adj_tiles[:, bass.ds(c * CT, CT), q * UC:(q + 1) * UC])\
                    .then_inc(adj_loaded[q], 16)

            sync.dma_start(w_in[:], w_rows).then_inc(const_loaded, 16)
            if linear:
                sync.dma_start(b_rows[:], b.rearrange("(o d) -> o d", o=1).to_broadcast([P, D])).then_inc(const_loaded, 16)
            for q in range(UNITS):
                load(0, q)

            def body(i, last):
                for k in range(2):
                    c = 2 * i + k
                    wait(sync, next_stored, 16 * c)
                    sync.dma_start(y[:], x_tiles[:, bass.ds(c * CT, CT), :]).then_inc(y_loaded, 16)
                    if not (last and k == 1):
                        for q in range(UNITS):
                            load(c + 1, q)
            paired_chunks(sync, body)
            sync.wait_ge(next_stored, 16 * CHUNKS)

        @block.gpsimd
        def _(pool):
            make_identity(pool, ident, ident_made)
            ln.constants(pool)

            def finish(c):
                ln.power(pool, c)
                pool.wait_ge(ln.norm_done, CT * (c + 1))
                pool.dma_start(next_tiles[:, bass.ds(c * CT, CT), :], y[:]).then_inc(next_stored, 16)
            finish(0)
            with pool.Fori(1, CHUNKS) as c:
                finish(c)

        @block.tensor
        def _(pe):
            pe.wait_ge(ident_made, 2)
            pe.wait_ge(const_loaded, 16 * CONST_LOADS)
            if linear:
                for half in range(DH):
                    for out in range(DH):
                        last = pe.transpose(rows_bank[half][:, out * P:(out + 1) * P],
                                            w_in[:, out, half * P:(half + 1) * P], ident[:])
                    last.then_inc(w_turned, 1)
                pe.wait_ge(w_ready, DH)

            def project(c):
                for half in range(DH):
                    pe.wait_ge(ag.outT_ready[half], c + 1)
                wait(pe, y_ready, c)
                for t in range(CT):
                    for half in range(DH):
                        last = pe.matmul(rows_bank[t // 2][:, t % 2 * D:(t % 2 + 1) * D],
                                         ag.outT[:, half, t * P:(t + 1) * P], w[:, half, :],
                                         start=half == 0, stop=half == DH - 1)
                last.then_inc(projected, 1)

            def body(i, last):
                for k in range(2):
                    c = 2 * i + k
                    has_before = not (isinstance(c, int) and c == 0)
                    for step in range(STEPS):
                        q, col = step // US, step % US * P
                        if step % US == 0:
                            pe.wait_ge(adj_loaded[q], 16 * (c + 1))
                        ag.turn(pe, c, step, [unit[:, q, t, col:col + P] for t in range(CT)])
                        if step >= LAG:
                            ag.multiply(pe, c, step - LAG, step - LAG)
                        elif has_before:
                            ag.multiply(pe, c - 1, STEPS + step - LAG, STEPS + step - LAG)
                        if step == 6 and has_before:
                            project(c - 1)
            paired_chunks(pe, body)
            for step in range(STEPS - LAG, STEPS):
                ag.multiply(pe, CHUNKS - 1, step, step)
            project(CHUNKS - 1)

        @block.scalar
        def _(act):
            def copy(out, in_):
                return act.activation(out, in_, ACT.Copy)

            def body(i, last):
                for k in range(2):
                    c = 2 * i + k
                    has_before = not (isinstance(c, int) and c == 0)
                    for step in range(STEPS):
                        ag.read_hi(act, c, step)
                        if step == 2 and has_before:
                            ag.keep_out(act, copy, 0, c - 1, projected)
            paired_chunks(act, body)
            ag.keep_out(act, copy, 0, CHUNKS - 1, projected)

        @block.vector
        def _(dve):
            dve.wait_ge(const_loaded, 16 * CONST_LOADS)
            if linear:
                for half in range(DH):
                    dve.wait_ge(w_turned, half + 1)
                    dve.tensor_copy(w[:, half, :], rows_bank[half][:, 0:D]).then_inc(w_ready, 1)

            def add_rows(c):
                dve.wait_ge(projected, c + 1)
                dve.wait_ge(y_loaded, 16 * (c + 1))
                dve.tensor_copy(scale[:], inv_deg[:, bass.ds(c * CT, CT)]).then_inc(scale_ready, 1)
                dve.wait_ge(scale_ready, c + 1)
                for t in range(CT):
                    rows = rows_bank[t // 2][:, t % 2 * D:(t % 2 + 1) * D]
                    if linear:
                        dve.scalar_tensor_tensor(out=relu[:, t, :], in0=rows, scalar=scale[:, t:t + 1], in1=b_rows[:],
                                                 op0=ALU.mult, op1=ALU.add).then_inc(relu_ready, 1)
                    else:
                        dve.tensor_scalar(relu[:, t, :], rows, scale[:, t:t + 1], 0.0, ALU.mult, ALU.max)\
                           .then_inc(relu_ready, 1)
                dve.wait_ge(relu_ready, CT * (c + 1))
                dve.tensor_tensor(y[:], y[:], relu[:], ALU.add).then_inc(y_ready, 1)
                dve.wait_ge(y_ready, c + 1)
                ln.statistics(dve, y, c)

            def body(i, last):
                for k in range(2):
                    c = 2 * i + k
                    has_before = not (isinstance(c, int) and c == 0)
                    for step in range(STEPS):
                        ag.read_lo(dve, c, step)
                        if step == 2 and has_before:
                            ag.keep_out(dve, dve.tensor_copy, 1, c - 1, projected)
                        if step == 9 and has_before:
                            add_rows(c - 1)
                        if step == 13 and has_before:
                            ln.normalise(dve, y, c - 1)
            paired_chunks(dve, body)
            ag.keep_out(dve, dve.tensor_copy, 1, CHUNKS - 1, projected)
            add_rows(CHUNKS - 1)
            ln.normalise(dve, y, CHUNKS - 1)


def build(nc, x, adj, Wqkv, bqkv, Wout, bout, graph_bias, W1, a1, W2, b2, W3, out):
    v_heads = nc.dram_tensor("v_heads", [H, P, NT, HD], F32, kind="Internal").ap()
    x1 = nc.dram_tensor("x1", [N, D], F32, kind="Internal").ap()
    x2 = nc.dram_tensor("x2", [N, D], F32, kind="Internal").ap()
    x3 = nc.dram_tensor("x3", [N, D], F32, kind="Internal").ap()
    value_stored = [nc.alloc_semaphore(f"value_stored{k}") for k in range(2)]
    x1_stored, x2_stored = nc.alloc_semaphore("x1_stored"), nc.alloc_semaphore("x2_stored")
    x3_stored, out_stored = nc.alloc_semaphore("x3_stored"), nc.alloc_semaphore("out_stored")
    with ExitStack() as ctx:
        kT = ctx.enter_context(nc.sbuf_tensor("kT", [P, H, N], F32R))
        layer0_keys_values(nc, x, Wqkv, bqkv, kT, v_heads, value_stored)
        used = layer0_attention(nc, x, adj, Wqkv, bqkv, Wout, bout, graph_bias, kT, v_heads, x1, x1_stored)
    with ExitStack() as ctx:
        inv_deg2 = ctx.enter_context(nc.sbuf_tensor("inv_deg2", [P, NT], F32))
        inv_deg3 = ctx.enter_context(nc.sbuf_tensor("inv_deg3", [P, NT], F32))
        values_hi = ctx.enter_context(nc.sbuf_tensor("values_hi", [P, NT * D], F32R))
        values_lo = ctx.enter_context(nc.sbuf_tensor("values_lo", [P, NT * D], F32R))
        with ExitStack() as inner:
            minus_src = inner.enter_context(nc.sbuf_tensor("minus_src", [P, NT], F32))
            dst_row = inner.enter_context(nc.sbuf_tensor("dst_row", [P, N], F32))
            layer1_values(nc, x1, W1, a1, values_hi, values_lo, minus_src, dst_row)
            layer1_attention(nc, x1, adj, values_hi, values_lo, minus_src, dst_row, inv_deg2, inv_deg3, x2, x2_stored)
        scaled_rows(nc, "s2", x2, inv_deg2, values_hi, values_lo)
        graph_convolution(nc, "g2", x2, adj, W2, b2, inv_deg2, values_hi, values_lo, x3, x3_stored)
        clear(nc, used)
        scaled_rows(nc, "s3", x3, inv_deg3, values_hi, values_lo, used)
        graph_convolution(nc, "g3", x3, adj, W3, None, inv_deg3, values_hi, values_lo, out, out_stored, used)


_INPUTS = ["x", "adj", "L0_gnn_Wqkv", "L0_gnn_bqkv", "L0_gnn_Wout", "L0_gnn_bout", "L0_gnn_graph_bias",
           "L1_gnn_W", "L1_gnn_a", "L2_gnn_W", "L2_gnn_b", "L3_gnn_W"]


def kernel(**inputs):
    import numpy as np
    from concourse import bacc
    from concourse.bass_utils import run_bass_kernel_spmd

    nc = bacc.Bacc("TRN2", target_bir_lowering=False, num_devices=1)
    arrays, args = {}, []
    for name in _INPUTS:
        a = np.ascontiguousarray(inputs[name])
        arrays[f"in_{name}"] = a
        args.append(nc.dram_tensor(f"in_{name}", a.shape, mybir.dt.from_np(a.dtype), kind="ExternalInput").ap())
    out = nc.dram_tensor("out", [N, D], F32, kind="ExternalOutput").ap()
    build(nc, *args, out)
    result = run_bass_kernel_spmd(nc, [arrays], core_ids=[0])
    return result.results[0]["out"]
```
